# Optimizing a Trainium2 kernel written in Bass

```python
import numpy as np
import jax
import jax.numpy as jnp

def _softmax(x, axis=-1):
    return jax.nn.softmax(x, axis=axis)

def _gelu(x):
    return jax.nn.gelu(x, approximate=True)

def _silu(x):
    return jax.nn.silu(x)

def _sigmoid(x):
    return jax.nn.sigmoid(x)

def _layernorm(x, axis=-1, eps=1e-05):
    m = jnp.mean(x, axis=axis, keepdims=True)
    v = jnp.var(x, axis=axis, keepdims=True)
    return (x - m) / jnp.sqrt(v + eps)

def _scatter_add(tgt, idx, src, axis=0):
    return tgt.at[idx].add(src)

def _segment_sum(src, seg, n):
    return jax.ops.segment_sum(src, seg, n)
kernel_name = 'mk_cond_resid_d4_seqx_r4_cec986'

def setup_inputs(seed: int=0):
    np.random.seed(seed)
    _w = jnp.asarray

    def _rec_inputs():
        import jax
        import jax.numpy as jnp
        _rk = jax.random.key(seed)
        x = -0.000125 + 0.9999 * jax.random.normal(jax.random.fold_in(_rk, 1), (8, 256, 1024), jnp.float32)
        _lenS = 256 - jax.random.randint(jax.random.fold_in(_rk, 7), (8,), 0, max(1, 256 // 4) + 1, jnp.int32)
        _lenS2 = 256 - jax.random.randint(jax.random.fold_in(_rk, 8), (8,), 0, max(1, 256 // 4) + 1, jnp.int32)
        itok_B_0_2 = jax.random.randint(jax.random.fold_in(_rk, 11), (8,), 0, 3, jnp.int32)
        condB_thresholds = jax.random.uniform(jax.random.fold_in(_rk, 12), (8,), jnp.float32, 0.0, 1.82799)
        condB_deltas = jax.random.uniform(jax.random.fold_in(_rk, 13), (8,), jnp.float32, 0.0, 0.0232459)
        condB_zeropoints = jax.random.uniform(jax.random.fold_in(_rk, 14), (8,), jnp.float32, 0.0, 243)
        itok_B_3_7 = jax.random.randint(jax.random.fold_in(_rk, 15), (8,), 3, 8, jnp.int32)
        return (x, itok_B_0_2, condB_thresholds, condB_deltas, condB_zeropoints, itok_B_3_7)
    x, itok_B_0_2, condB_thresholds, condB_deltas, condB_zeropoints, itok_B_3_7 = _rec_inputs()

    def _L0_cond_setup():
        import jax, jax.numpy as jnp
        import numpy as np
        B, S, D_IN, D_OUT = (4, 512, 1024, 1024)
        R, NUM_LABELERS = (32, 5)
        LORA_SCALING = 16 / 32
        key = jax.random.key(seed)
        k1, k2, k3, k4, k5 = jax.random.split(key, 5)
        x = jax.random.normal(k1, (B, S, D_IN), dtype=jnp.float32)
        labeler_index = jax.random.randint(k2, (B,), 0, NUM_LABELERS, dtype=jnp.int64)
        W = jax.random.normal(k3, (D_OUT, D_IN), dtype=jnp.float32) * 0.02
        lora_A = jax.random.normal(k4, (NUM_LABELERS, D_IN, R), dtype=jnp.float32) * 0.02
        lora_B_w = jax.random.normal(k5, (D_OUT, R), dtype=jnp.float32) * 0.02
        return {'x': x, 'labeler_index': labeler_index, 'W': W, 'lora_A': lora_A, 'lora_B_w': lora_B_w}
    _L0_cond_all = _L0_cond_setup()
    _L0_cond_in = {k: v for k, v in _L0_cond_all.items() if k in ('W', 'lora_A', 'lora_B_w')}
    del _L0_cond_all

    def _L1_cond_setup():
        import jax, jax.numpy as jnp
        import numpy as np
        N_LEVELS = 64
        key = jax.random.key(seed)
        k1, k2, k3, k4 = jax.random.split(key, 4)
        x = jax.random.normal(k1, (4, 1024, 1024), dtype=jnp.float32)
        G = 4
        thresholds = jnp.sort(jax.random.uniform(k2, (G,), minval=0.2, maxval=3.0))[::-1].astype(jnp.float32)
        deltas = (jax.random.uniform(k3, (G,)) * 0.02 + 0.005).astype(jnp.float32)
        zero_points = jnp.round(jax.random.uniform(k4, (G,)) * (N_LEVELS - 1)).astype(jnp.float32)
        return {'x': x, 'thresholds': thresholds, 'deltas': deltas, 'zero_points': zero_points}
    _L1_cond_all = _L1_cond_setup()
    _L1_cond_in = {k: v for k, v in _L1_cond_all.items() if k in ()}
    del _L1_cond_all

    def _L2_cond_setup():
        import jax, jax.numpy as jnp
        import numpy as np
        MAX_LORAS, OUT, IN = (8, 1024, 1024)
        B, S = (4, 512)
        key = jax.random.key(seed)
        k1, k2, k3 = jax.random.split(key, 3)
        x = jax.random.normal(k1, (B, S, IN), dtype=jnp.float32)
        weight = jax.random.normal(k2, (MAX_LORAS, OUT, IN), dtype=jnp.float32) * 0.02
        adapter_ids = jax.random.randint(k3, (B,), 0, MAX_LORAS, dtype=jnp.int32)
        return {'x': x, 'weight': weight, 'adapter_ids': adapter_ids}
    _L2_cond_all = _L2_cond_setup()
    _L2_cond_in = {k: v for k, v in _L2_cond_all.items() if k in ('weight',)}
    del _L2_cond_all

    def _L3_cond_setup():
        import jax, jax.numpy as jnp
        import numpy as np
        RANK = 16
        ALPHA = 16.0
        SCALING = ALPHA / RANK
        N_ADAPTERS = 8
        IN_F = 1024
        OUT_F = 1024
        BATCH = 4
        SEQ = 512
        key = jax.random.key(seed)
        kx, ka, kb, ki = jax.random.split(key, 4)
        x = jax.random.normal(kx, (BATCH, SEQ, IN_F), dtype=jnp.float32)
        A = jax.random.normal(ka, (N_ADAPTERS, OUT_F, RANK), dtype=jnp.float32) * 0.02
        B = jax.random.normal(kb, (N_ADAPTERS, RANK, IN_F), dtype=jnp.float32) * 0.02
        adapter_ids = jax.random.randint(ki, (BATCH,), 0, N_ADAPTERS, dtype=jnp.int32)
        return {'x': x, 'A': A, 'B': B, 'adapter_ids': adapter_ids}
    _L3_cond_all = _L3_cond_setup()
    _L3_cond_in = {k: v for k, v in _L3_cond_all.items() if k in ('A', 'B')}
    del _L3_cond_all
    return {'x': x, 'itok_B_0_2': itok_B_0_2, 'condB_thresholds': condB_thresholds, 'condB_deltas': condB_deltas, 'condB_zeropoints': condB_zeropoints, 'itok_B_3_7': itok_B_3_7, 'L0_cond_W': _L0_cond_in['W'], 'L0_cond_lora_A': _L0_cond_in['lora_A'], 'L0_cond_lora_B_w': _L0_cond_in['lora_B_w'], 'L2_cond_weight': _L2_cond_in['weight'], 'L3_cond_A': _L3_cond_in['A'], 'L3_cond_B': _L3_cond_in['B']}

def reference(x, itok_B_0_2, condB_thresholds, condB_deltas, condB_zeropoints, itok_B_3_7, L0_cond_W, L0_cond_lora_A, L0_cond_lora_B_w, L2_cond_weight, L3_cond_A, L3_cond_B):
    import jax
    import jax.numpy as jnp

    def _L0_cond_ref(x, labeler_index, W, lora_A, lora_B_w):
        import jax, jax.numpy as jnp
        import numpy as np
        B, S, D_IN, D_OUT = (4, 512, 1024, 1024)
        R, NUM_LABELERS = (32, 5)
        LORA_SCALING = 16 / 32
        base = jnp.einsum('bsi,oi->bso', x, W)
        labelers_A = lora_A[labeler_index]
        low = jnp.einsum('bsi,bir->bsr', x, labelers_A)
        delta = jnp.einsum('bsr,or->bso', low, lora_B_w) * LORA_SCALING
        return base + delta

    def _L1_cond_ref(x, thresholds, deltas, zero_points):
        import jax, jax.numpy as jnp
        import numpy as np
        N_LEVELS = 64
        G = thresholds.shape[0]
        gi = jnp.sum(jnp.abs(x)[..., None] <= thresholds, axis=-1)
        idx = jnp.minimum(gi, G - 1)
        d = deltas[idx]
        zp = zero_points[idx]
        x_quant = jnp.clip(jnp.round(x / d) + zp, 0, N_LEVELS - 1)
        x_dequant = (x_quant - zp) * d
        return jnp.where(gi == G, jnp.float32(0), x_dequant)

    def _L2_cond_ref(x, weight, adapter_ids):
        import jax, jax.numpy as jnp
        import numpy as np
        MAX_LORAS, OUT, IN = (8, 1024, 1024)
        B, S = (4, 512)
        w = weight[adapter_ids]
        return jnp.einsum('bsi,boi->bso', x, w)

    def _L3_cond_ref(x, A, B, adapter_ids):
        import jax, jax.numpy as jnp
        import numpy as np
        RANK = 16
        ALPHA = 16.0
        SCALING = ALPHA / RANK
        N_ADAPTERS = 8
        IN_F = 1024
        OUT_F = 1024
        BATCH = 4
        SEQ = 512
        B_sel = B[adapter_ids]
        A_sel = A[adapter_ids]
        Bx = jnp.einsum('bni,bri->bnr', x, B_sel)
        out = jnp.einsum('bnr,bor->bno', Bx, A_sel)
        return out * SCALING
    x = x + _L0_cond_ref(x, itok_B_0_2, L0_cond_W, L0_cond_lora_A, L0_cond_lora_B_w)
    x = x + _L1_cond_ref(x, condB_thresholds, condB_deltas, condB_zeropoints)
    x = x + _L2_cond_ref(x, L2_cond_weight, itok_B_3_7)
    x = x + _L3_cond_ref(x, L3_cond_A, L3_cond_B, itok_B_3_7)
    return x

_drawn_inputs = setup_inputs


def setup_inputs(seed=0):
    import zlib

    import numpy as np

    out = dict(_drawn_inputs(seed))
    spreads = {}
    factors = {}
    for name, (base, spread) in spreads.items():
        noise = np.random.default_rng([zlib.crc32(name.encode()), seed]).standard_normal(out[name].shape)
        drawn = base * np.exp(spread * noise) if base else spread * noise
        out[name] = jnp.asarray(drawn.astype(out[name].dtype))
    for name, factor in factors.items():
        out[name] = (out[name] * factor).astype(out[name].dtype)
    return out
```

```python
from contextlib import ExitStack

import concourse.bass as bass
import numpy as np
from concourse import mybir

ALU = mybir.AluOpType
ACT = mybir.ActivationFunctionType
F32 = mybir.dt.float32
F32R = mybir.dt.float32r
BF16 = mybir.dt.bfloat16
I16 = mybir.dt.int16
I32 = mybir.dt.int32

P = 128
B, S, D = 8, 256, 1024
T = D // P
BW = T * S
UW = BW // 2
CW = BW // 4
QUAD = 32
R0 = 32
R3 = 16
G = 8
TOP_LEVEL = 63.0
ROUND = 12582912.0
STEEP = 2.0 ** 40
BELOW_ONE = 1.0 - 2.0 ** -24
POOL_GROUPS = (1, 3, 5, 7)


def build(nc, x, labels, adapters, thresholds, deltas, zeropoints, w0, a0, b0, w2, b3, a3, out):
    with ExitStack() as ctx:
        def sb(name, shape, dt):
            return ctx.enter_context(nc.sbuf_tensor(name, shape, dt))

        def ps(name, shape):
            return ctx.enter_context(nc.psum_tensor(name, shape, F32))

        def sem(name):
            return ctx.enter_context(nc.semaphore(name))

        w0_hi = sb("w0_hi", [P, T, T * P], F32R)
        w0_lo = sb("w0_lo", [P, T, T * P], F32R)
        w2_sb = sb("w2_sb", [P, T, T * P], F32)
        x_raw = sb("x_raw", [P, BW], F32)
        x_hi = sb("x_hi", [P, 2, BW], F32R)
        x_lo = sb("x_lo", [P, 2, BW], F32R)
        a0_raw = sb("a0_raw", [P, T, R0], F32)
        a0_split = sb("a0_split", [P, T, 4, R0], F32R)
        b0_split = sb("b0_split", [P, D], F32R)
        low_split = sb("low_split", [P, S], F32R)
        magnitude = sb("magnitude", [P, UW], F32)
        cand = sb("cand", [P, 4, UW], F32)
        mask = sb("mask", [P, 4, UW], BF16)
        x2 = sb("x2", [P, 2, BW], F32)
        x3 = sb("x3", [P, 2, BW], F32)
        b3_raw = sb("b3_raw", [P, T, R3], F32)
        b3_wide = sb("b3_wide", [P, T, 4, QUAD], F32)
        a3_raw = sb("a3_raw", [P, D], F32)
        a3_split = sb("a3_split", [P, D], F32R)
        bx_split = sb("bx_split", [P, S], F32R)
        ident = sb("ident", [P, P], F32)
        zero = sb("zero", [P, 1], F32)
        ez = sb("ez", [P, 1], F32)
        thr = sb("thr", [P, G], F32)
        delta = sb("delta", [P, G], F32)
        zp = sb("zp", [P, G], F32)
        sorted_thr = sb("sorted_thr", [P, G], F32)
        thr_bias = sb("thr_bias", [P, G], F32)
        inv_delta = sb("inv_delta", [P, G], F32)
        top = sb("top", [P, G], F32)
        lower = sb("lower", [P, G], F32)
        upper = sb("upper", [P, G], F32)
        label_ids = sb("label_ids", [1, B], I32)
        adapter_ids = sb("adapter_ids", [1, B], I32)

        l0_ps = ps("l0_ps", [P, 2, UW])
        l2_ps = ps("l2_ps", [P, 2, CW])
        l3_ps = ps("l3_ps", [P, CW])
        bx_ps = ps("bx_ps", [P, CW])

        params_loaded = sem("params_loaded")
        b0_loaded = sem("b0_loaded")
        w0_loaded = [sem(f"w0_loaded{o}") for o in range(T)]
        x_loaded = sem("x_loaded")
        a0_loaded = sem("a0_loaded")
        w2_loaded = [sem(f"w2_loaded{q}") for q in range(4)]
        b3_loaded = sem("b3_loaded")
        a3_loaded = sem("a3_loaded")
        out_stored = [sem(f"out_stored{q}") for q in range(4)]
        ident_zeroed = sem("ident_zeroed")
        ident_ready = sem("ident_ready")
        gaps_zeroed = sem("gaps_zeroed")
        param_step = sem("param_step")
        sp_waited = sem("sp_waited")
        dve_waited = sem("dve_waited")
        pool_waited = sem("pool_waited")
        diag_added = sem("diag_added")
        w0_hi_done = sem("w0_hi_done")
        w0_split_done = sem("w0_split_done")
        b0_hi_done = sem("b0_hi_done")
        b0_split_done = sem("b0_split_done")
        x_hi_done = sem("x_hi_done")
        x_split_done = sem("x_split_done")
        low_done = sem("low_done")
        low_hi_done = sem("low_hi_done")
        low_split_done = sem("low_split_done")
        l0_done = sem("l0_done")
        mag_done = sem("mag_done")
        rounded = sem("rounded")
        masked = sem("masked")
        scaled_dve = sem("scaled_dve")
        scaled_pool = sem("scaled_pool")
        clipped = sem("clipped")
        merged = sem("merged")
        zeroed = sem("zeroed")
        x2_done = sem("x2_done")
        l2_done = sem("l2_done")
        x3_done = sem("x3_done")
        b3_done = sem("b3_done")
        a3_hi_done = sem("a3_hi_done")
        a3_split_done = sem("a3_split_done")
        bx_done = sem("bx_done")
        bx_hi_done = sem("bx_hi_done")
        bx_split_done = sem("bx_split_done")
        l3_done = sem("l3_done")
        out_done = sem("out_done")

        pool_share = len(POOL_GROUPS)
        dve_share = G - pool_share

        def all_steps(engine, step):
            step(0, 0, True, False, False)
            step(1, 1, True, True, False)
            with engine.Fori(1, B // 2) as pair:
                s = pair * 2
                step(s, 0, True, True, True)
                step(s + 1, 1, True, True, True)
            step(B, 0, False, True, True)
            step(B + 1, 1, False, False, True)

        def first(s):
            return isinstance(s, int) and s == 0

        block = ctx.enter_context(nc.Block())

        @block.sync
        def _(sp):
            def load_x(n):
                sp.dma_start(x_raw[:, :], x[bass.ds(n, 1)].rearrange("b p w -> p (b w)")).then_inc(x_loaded, 16)

            def load_a0(n):
                label = sp.value_load(label_ids[0:1, bass.ds(n, 1)], min_val=0, max_val=a0.shape[0] - 1)
                sp.dma_start(a0_raw[:, :, :].rearrange("p k r -> p (k r)"),
                             a0[bass.ds(label, 1)].rearrange("l p w -> p (l w)")).then_inc(a0_loaded, 16)

            for q in range(4):
                sp.sem_inc(out_stored[q], 1)
            sp.dma_start(label_ids[:, :], labels.rearrange("(a n) -> a n", a=1)).then_inc(params_loaded, 16)
            sp.dma_start(adapter_ids[:, :], adapters.rearrange("(a n) -> a n", a=1)).then_inc(params_loaded, 16)
            for dst, src in ((thr, thresholds), (delta, deltas), (zp, zeropoints)):
                sp.dma_start(dst[:, :], src.rearrange("(a n) -> a n", a=1).to_broadcast([P, G]))\
                  .then_inc(params_loaded, 16)
            load_x(0)
            sp.dma_start(w2_sb[:, 0, :], w0[0]).then_inc(w0_loaded[0], 16)
            sp.wait_ge(params_loaded, 5 * 16)
            load_a0(0)
            sp.dma_start(w2_sb[:, 1, :], w0[1]).then_inc(w0_loaded[1], 16)
            for q in range(4):
                sp.dma_start(a3_raw[q * QUAD:(q + 1) * QUAD, :], b0).then_inc(b0_loaded, 16)
            for o in range(2, T):
                sp.dma_start(w2_sb[:, o, :], w0[o]).then_inc(w0_loaded[o], 16)

            def step(s, parity, stage_a, stage_b, stage_c):
                if stage_a:
                    sp.wait_ge(x_split_done, s + 1)
                    sp.sem_inc(sp_waited, 1)
                    load_x((s + 1) % B)
                    load_a0((s + 1) % B)
                if stage_b:
                    adapter = sp.value_load(adapter_ids[0:1, bass.ds(s - 1, 1)], min_val=0, max_val=b3.shape[0] - 1)
                    if stage_c:
                        sp.wait_ge(b3_done, s - 1)
                        sp.sem_inc(sp_waited, 1)
                        sp.wait_ge(a3_split_done, (s - 1) * 2)
                        sp.sem_inc(sp_waited, 1)
                    else:
                        sp.wait_ge(gaps_zeroed, 2)
                    sp.dma_start(b3_raw[:, :, :].rearrange("p k r -> p (k r)"),
                                 b3[bass.ds(adapter, 1)].rearrange("l p w -> p (l w)")).then_inc(b3_loaded, 16)
                    for q in range(4):
                        sp.dma_start(a3_raw[q * QUAD:q * QUAD + R3, :],
                                     a3[bass.ds(adapter, 1)].rearrange("l r w -> r (l w)")).then_inc(a3_loaded, 16)
                if stage_a:
                    adapter = sp.value_load(adapter_ids[0:1, bass.ds(s, 1)], min_val=0, max_val=b3.shape[0] - 1)
                for q in range(4):
                    if stage_a:
                        if first(s):
                            sp.wait_ge(w0_split_done, 2 * q + 2)
                        else:
                            sp.wait_ge(l2_done, (s - 1) * 4 + (q + 1))
                            sp.sem_inc(sp_waited, 1)
                        sp.dma_start(w2_sb[:, 2 * q:2 * q + 2, :],
                                     w2[bass.ds(adapter, 1), q].rearrange("l p o w -> p (l o) w"))\
                          .then_inc(w2_loaded[q], 16)
                    if stage_c:
                        sp.wait_ge(out_done, (s - 2) * 4 + (q + 1))
                        sp.sem_inc(sp_waited, 1)
                        sp.dma_start(out[bass.ds(s - 2, 1), q].rearrange("b p w -> p (b w)"),
                                     x3[:, parity, q * CW:(q + 1) * CW]).then_inc(out_stored[q], 16)

            all_steps(sp, step)
            for q in range(4):
                sp.wait_ge(out_stored[q], 16 * B + 1)

        @block.gpsimd
        def _(pool):
            pool.memset(ident[:, :], 0.0).then_inc(ident_zeroed, 1)
            pool.wait_ge(ident_zeroed, 1)
            pool.affine_select(out=ident[:, :], in_=ident[:, :], compare_op=ALU.not_equal, fill=1.0,
                               base=0, pattern=[[-1, P]], channel_multiplier=1).then_inc(ident_ready, 1)
            pool.memset(zero[:, :], 0.0).then_inc(ident_ready, 1)
            pool.memset(b3_wide[:, :, :, :], 0.0).then_inc(gaps_zeroed, 1)
            pool.wait_ge(b0_split_done, 1)
            pool.memset(a3_raw[:, :], 0.0).then_inc(gaps_zeroed, 1)

            def rescale(s, half):
                for n, k in enumerate(POOL_GROUPS):
                    c = cand[:, k % 4, :]
                    pool.wait_ge(rounded, (s * 2 + half) * G + (k + 1))
                    pool.sem_inc(pool_waited, 1)
                    pool.tensor_scalar(c, c, -ROUND, delta[:, k:k + 1], ALU.add, ALU.mult)\
                        .then_inc(scaled_pool, 1)

            def step(s, parity, stage_a, stage_b, stage_c):
                if stage_c:
                    pool.wait_ge(b3_loaded, (s - 1) * 16)
                    if not stage_b:
                        pool.wait_ge(bx_done, s - 2)
                    pool.sem_inc(pool_waited, 1)
                    pool.tensor_copy(b3_wide[:, :, :, 0:R3],
                                     b3_raw[:, :, :].unsqueeze(2).to_broadcast([P, T, 4, R3])).then_inc(b3_done, 1)
                    pool.wait_ge(a3_hi_done, s - 1)
                    pool.wait_ge(b3_done, s - 1)
                    for n, q in enumerate((1, 3)):
                        rows = slice(q * QUAD, q * QUAD + R3)
                        pool.tensor_tensor(a3_split[rows, :], a3_raw[rows, :],
                                           a3_split[rows, :].bitcast(F32), ALU.subtract)\
                            .then_inc(a3_split_done, 1)
                        pool.wait_ge(a3_split_done, (s - 2) * 2 + (n + 1))
                if stage_a:
                    rescale(s, 0)
                    rescale(s, 1)

            pool.wait_ge(params_loaded, 5 * 16)
            all_steps(pool, step)

        @block.scalar
        def _(act):
            def split_batch(s, parity):
                act.wait_ge(x_loaded, (s + 1) * 16)
                act.wait_ge(a0_loaded, (s + 1) * 16)
                act.activation(a0_split[:, :, :, :], a0_raw[:, :, :].unsqueeze(2).to_broadcast([P, T, 4, R0]),
                               ACT.Copy).then_inc(x_hi_done, 1)
                act.activation(x_hi[:, parity, :], x_raw[:, :], ACT.Copy).then_inc(x_hi_done, 1)

            def low_rank_hi(s):
                act.wait_ge(low_done, s + 1)
                if not first(s):
                    act.wait_ge(l0_done, s * 2)
                act.activation(low_split[:, :], bx_ps[:, 0:S], ACT.Copy).then_inc(low_hi_done, 1)

            act.wait_ge(ident_ready, 2)
            act.activation(ez[:, :], zero[:, :], ACT.Abs)
            split_batch(0, 0)
            for o in range(T):
                act.wait_ge(diag_added, o + 1)
                act.activation(w0_hi[:, o, :], w2_sb[:, o, :], ACT.Copy).then_inc(w0_hi_done, 1)
                if o == 0:
                    act.wait_ge(b0_loaded, 4 * 16)
                    act.activation(b0_split[:, :], a3_raw[:, :], ACT.Copy, scale=0.5).then_inc(b0_hi_done, 1)
                if o == 1:
                    low_rank_hi(0)

            def quantise(s, half):
                unit = s * 2 + half
                src = l0_ps[:, half, :]
                act.wait_ge(l0_done, unit + 1)
                if not (first(s) and half == 0):
                    act.wait_ge(masked, unit * G)
                act.activation(magnitude[:, :], src, ACT.Abs).then_inc(mag_done, 1)

                def candidate(k):
                    if not (first(s) and half == 0 and k < 4):
                        act.wait_ge(merged, unit * G + (k - 3))
                    act.activation(cand[:, k % 4, :], src, ACT.Identity, bias=ROUND,
                                   scale=inv_delta[:, k:k + 1]).then_inc(rounded, 1)

                def test(j):
                    if not (first(s) and half == 0 and j < 4):
                        if j == 3:
                            act.wait_ge(x2_done, unit)
                        else:
                            act.wait_ge(merged, unit * G + (j - 2))
                    act.activation(mask[:, j % 4, :], magnitude[:, :], ACT.Relu, bias=thr_bias[:, j:j + 1],
                                   scale=-STEEP * BELOW_ONE).then_inc(masked, 1)

                candidate(0)
                candidate(1)
                act.wait_ge(mag_done, unit + 1)
                for k in range(2, G):
                    test(k - 2)
                    candidate(k)
                    if k == 6 and half == 1:
                        low_rank_hi(s + 1)
                test(G - 2)
                test(G - 1)

            def step(s, parity, stage_a, stage_b, stage_c):
                if stage_c:
                    act.wait_ge(a3_loaded, (s - 1) * 64)
                    act.wait_ge(l2_done, (s - 1) * 4)
                    act.activation(a3_split[:, :], a3_raw[:, :], ACT.Copy).then_inc(a3_hi_done, 1)
                if stage_c:
                    act.wait_ge(bx_done, s - 1)
                    act.activation(bx_split[:, :], bx_ps[:, 0:S], ACT.Copy).then_inc(bx_hi_done, 1)
                if stage_a:
                    quantise(s, 0)
                    if not first(s):
                        act.wait_ge(l0_done, s * 2)
                    split_batch(s + 1, 1 - parity)
                    quantise(s, 1)

            act.wait_ge(param_step, 7)
            all_steps(act, step)

        @block.vector
        def _(dve):
            def split_batch(s, parity):
                dve.wait_ge(x_hi_done, s * 2 + 1)
                dve.tensor_tensor(a0_split[:, :, 2, :], a0_raw[:, :, :], a0_split[:, :, 2, :].bitcast(F32),
                                  ALU.subtract)
                dve.wait_ge(x_hi_done, s * 2 + 2)
                dve.tensor_tensor(x_lo[:, parity, :], x_raw[:, :], x_hi[:, parity, :].bitcast(F32),
                                  ALU.subtract).then_inc(x_split_done, 1)

            def low_rank_lo(s):
                rows = slice(3 * QUAD, 4 * QUAD)
                dve.wait_ge(low_hi_done, s + 1)
                dve.tensor_tensor(low_split[rows, :], bx_ps[rows, 0:S], low_split[rows, :].bitcast(F32),
                                  ALU.subtract).then_inc(low_split_done, 1)

            dve.wait_ge(params_loaded, 5 * 16)
            dve.max(sorted_thr[:, :], thr[:, :]).then_inc(param_step, 1)
            dve.reciprocal(inv_delta[:, :], delta[:, :]).then_inc(param_step, 1)
            dve.tensor_scalar(top[:, :], zp[:, :], -1.0, TOP_LEVEL, ALU.mult, ALU.add).then_inc(param_step, 1)
            dve.scalar_tensor_tensor(lower[:, :], zp[:, :], -1.0, delta[:, :], ALU.mult, ALU.mult)\
                .then_inc(param_step, 1)
            dve.wait_ge(param_step, 3)
            dve.tensor_tensor(upper[:, :], top[:, :], delta[:, :], ALU.mult).then_inc(param_step, 1)
            dve.tensor_scalar(thr_bias[:, :], sorted_thr[:, :], STEEP, 1e-30, ALU.mult, ALU.add)\
                .then_inc(param_step, 1)
            dve.wait_ge(ident_ready, 2)
            dve.wait_ge(w0_loaded[0], 16)

            def add_diag(o):
                dve.wait_ge(w0_loaded[o], 16)
                d = w2_sb[:, o, o * P:(o + 1) * P]
                dve.tensor_tensor(d, d, ident[:, :], ALU.add).then_inc(diag_added, 1)

            add_diag(0)
            dve.wait_ge(param_step, 6)
            dve.tensor_copy(top[:, :], upper[:, :]).then_inc(param_step, 1)
            split_batch(0, 0)
            for o in range(T):
                if o + 1 < T:
                    add_diag(o + 1)
                dve.wait_ge(w0_hi_done, o + 1)
                dve.tensor_tensor(w0_lo[:, o, :], w2_sb[:, o, :], w0_hi[:, o, :].bitcast(F32),
                                  ALU.subtract).then_inc(w0_split_done, 1)
                if o == 0:
                    rows = slice(QUAD, 2 * QUAD)
                    dve.wait_ge(b0_hi_done, 1)
                    dve.scalar_tensor_tensor(b0_split[rows, :], a3_raw[rows, :], 0.5,
                                             b0_split[rows, :].bitcast(F32), ALU.mult, ALU.subtract)\
                        .then_inc(b0_split_done, 1)
                if o == 1:
                    low_rank_lo(0)

            def finish_chunk(s, parity, q, stage_c):
                cols = slice(q * CW, (q + 1) * CW)
                if stage_c:
                    dve.wait_ge(out_stored[q], (s - 2) * 16 + 1)
                    dve.wait_ge(l3_done, (s - 2) * 4 + (q + 1))
                    dve.tensor_tensor(x3[:, parity, cols], l3_ps[:, :], x3[:, parity, cols], ALU.add)\
                       .then_inc(out_done, 1)

            def drain_chunk(s, parity, q, stage_b):
                cols = slice(q * CW, (q + 1) * CW)
                if stage_b:
                    dve.wait_ge(l2_done, (s - 1) * 4 + (q + 1))
                    dve.tensor_tensor(x3[:, 1 - parity, cols], l2_ps[:, q % 2, :], x2[:, 1 - parity, cols],
                                      ALU.add).then_inc(x3_done, 1)

            def quantise(s, half, parity, stage_b, stage_c):
                unit = s * 2 + half
                y = x2[:, parity, half * UW:(half + 1) * UW]

                def scale(k):
                    if k not in POOL_GROUPS:
                        c = cand[:, k % 4, :]
                        dve.wait_ge(rounded, unit * G + (k + 1))
                        dve.tensor_scalar(c, c, -ROUND, delta[:, k:k + 1], ALU.add, ALU.mult)\
                            .then_inc(scaled_dve, 1)

                def clip(k):
                    c = cand[:, k % 4, :]
                    before = sum(1 for n in POOL_GROUPS if n < k)
                    if k in POOL_GROUPS:
                        dve.wait_ge(scaled_pool, unit * pool_share + (before + 1))
                    else:
                        dve.wait_ge(scaled_dve, unit * dve_share + (k - before + 1))
                    if k == 0:
                        dve.tensor_scalar(y, c, lower[:, k:k + 1], upper[:, k:k + 1], ALU.max, ALU.min)\
                            .then_inc(merged, 1)
                    else:
                        dve.tensor_scalar(c, c, lower[:, k:k + 1], upper[:, k:k + 1], ALU.max, ALU.min)\
                            .then_inc(clipped, 1)

                def merge(k):
                    dve.wait_ge(masked, unit * G + k)
                    dve.wait_ge(clipped, unit * (G - 1) + k)
                    dve.sem_inc(dve_waited, 1)
                    dve.copy_predicated(y, mask[:, (k - 1) % 4, :].bitcast(I16), cand[:, k % 4, :])\
                        .then_inc(merged, 1)

                if not (isinstance(s, int) and s < 2):
                    dve.wait_ge(x3_done, (s - 1) * 4)
                finish_chunk(s, parity, 2 * half, stage_c)
                scale(0)
                scale(1)
                clip(0)
                clip(1)
                for k in range(2, G):
                    scale(k)
                    dve.wait_ge(merged, unit * G + (k - 1))
                    merge(k - 1)
                    clip(k)
                    if k == 4:
                        drain_chunk(s, parity, 2 * half, stage_b)
                        finish_chunk(s, parity, 2 * half + 1, stage_c)
                    if k == 6:
                        drain_chunk(s, parity, 2 * half + 1, stage_b)
                        if half == 1:
                            low_rank_lo(s + 1)
                dve.wait_ge(merged, unit * G + (G - 1))
                merge(G - 1)
                dve.wait_ge(masked, unit * G + G)
                dve.wait_ge(merged, unit * G + G)
                dve.sem_inc(dve_waited, 1)
                dve.copy_predicated(y, mask[:, (G - 1) % 4, :].bitcast(I16), zero[:, :].to_broadcast([P, UW]))\
                    .then_inc(zeroed, 1)
                dve.wait_ge(zeroed, unit + 1)
                dve.tensor_tensor(y, l0_ps[:, half, :], y, ALU.add).then_inc(x2_done, 1)

            def step(s, parity, stage_a, stage_b, stage_c):
                if stage_c:
                    rows = slice(2 * QUAD, 4 * QUAD)
                    dve.wait_ge(bx_hi_done, s - 1)
                    dve.tensor_tensor(bx_split[rows, :], bx_ps[rows, 0:S], bx_split[rows, :].bitcast(F32),
                                      ALU.subtract).then_inc(bx_split_done, 1)
                if stage_a:
                    quantise(s, 0, parity, stage_b, stage_c)
                    split_batch(s + 1, 1 - parity)
                    quantise(s, 1, parity, stage_b, stage_c)
                else:
                    for q in range(4):
                        finish_chunk(s, parity, q, stage_c)
                        drain_chunk(s, parity, q, stage_b)

            all_steps(dve, step)

        @block.tensor
        def _(pe):
            def layer0(s, parity, half, tiles):
                for i in tiles:
                    o = half * (T // 2) + i
                    dst = l0_ps[:, half, i * S:(i + 1) * S]
                    if i == 0 and not first(s):
                        pe.wait_ge(x2_done, s * 2 + (half - 1))
                    if first(s):
                        pe.wait_ge(w0_split_done, o + 1)
                    start = True
                    for w, v in ((w0_hi, x_hi), (w0_lo, x_hi), (w0_hi, x_lo)):
                        for k in range(T):
                            nc.tensor.matmul(dst, w[:, o, k * P:(k + 1) * P], v[:, parity, k * S:(k + 1) * S],
                                             start=start, stop=False)
                            start = False
                    if half == 0 and i == 0:
                        pe.wait_ge(low_split_done, s + 1)
                        if first(s):
                            pe.wait_ge(b0_split_done, 1)
                    last = nc.tensor.matmul(dst, b0_split[:, o * P:(o + 1) * P], low_split[:, :],
                                            start=False, stop=True)
                if i == T // 2 - 1:
                    last.then_inc(l0_done, 1)

            def low_rank0(s, parity):
                pe.wait_ge(x_split_done, s + 1)
                for v in (x_hi, x_lo):
                    for k in range(T):
                        last = nc.tensor.matmul(bx_ps[:, 0:S], a0_split[:, k, :, :].rearrange("p q r -> p (q r)"),
                                                v[:, parity, k * S:(k + 1) * S],
                                                start=(v is x_hi and k == 0), stop=(v is x_lo and k == T - 1))
                last.then_inc(low_done, 1)

            def low_rank3(s, parity):
                pe.wait_ge(x3_done, (s - 1) * 4)
                pe.wait_ge(b3_done, s - 1)
                if isinstance(s, int) and s == B:
                    pe.wait_ge(low_split_done, B + 1)
                for k in range(T):
                    last = nc.tensor.matmul(bx_ps[:, 0:S], b3_wide[:, k, :, :].rearrange("p q r -> p (q r)"),
                                            x3[:, parity, k * S:(k + 1) * S], start=(k == 0), stop=(k == T - 1))
                last.then_inc(bx_done, 1)

            def step(s, parity, stage_a, stage_b, stage_c):
                if stage_a:
                    layer0(s, parity, 0, range(0, 2))
                if stage_c:
                    low_rank3(s, parity)
                if stage_a:
                    layer0(s, parity, 0, range(2, 4))
                for q in range(4):
                    if q == 2 and stage_a:
                        layer0(s, parity, 1, range(4))
                    if q == 3 and stage_a:
                        low_rank0(s + 1, 1 - parity)
                    if stage_c:
                        if q == 0:
                            pe.wait_ge(bx_split_done, s - 1)
                            pe.wait_ge(a3_split_done, (s - 1) * 2)
                        else:
                            pe.wait_ge(out_done, (s - 2) * 4 + q)
                        for i in range(2):
                            o = 2 * q + i
                            last = nc.tensor.matmul(l3_ps[:, i * S:(i + 1) * S], a3_split[:, o * P:(o + 1) * P],
                                                    bx_split[:, :], start=True, stop=True)
                        last.then_inc(l3_done, 1)
                    if stage_b:
                        pe.wait_ge(w2_loaded[q], s * 16)
                        if q == 0:
                            pe.wait_ge(x2_done, s * 2)
                        if not (isinstance(s, int) and s == 1 and q < 2):
                            pe.wait_ge(x3_done, (s - 1) * 4 + (q - 1))
                        for i in range(2):
                            o = 2 * q + i
                            for k in range(T):
                                last = nc.tensor.matmul(l2_ps[:, q % 2, i * S:(i + 1) * S],
                                                        w2_sb[:, o, k * P:(k + 1) * P],
                                                        x2[:, 1 - parity, k * S:(k + 1) * S],
                                                        start=(k == 0), stop=(k == T - 1))
                        last.then_inc(l2_done, 1)

            low_rank0(0, 0)
            all_steps(pe, step)


def kernel(x, itok_B_0_2, condB_thresholds, condB_deltas, condB_zeropoints, itok_B_3_7, L0_cond_W,
           L0_cond_lora_A, L0_cond_lora_B_w, L2_cond_weight, L3_cond_A, L3_cond_B):
    import concourse.bacc as bacc
    from concourse.bass_utils import run_bass_kernel_spmd

    def tiles_of_weights(w):
        w = np.asarray(w)
        lead = w.shape[:-2]
        n = len(lead)
        w = w.reshape(*lead, T, P, T, P)
        return np.ascontiguousarray(w.transpose(*range(n), n, n + 3, n + 2, n + 1)).reshape(*lead, T, P, T * P)

    x = np.asarray(x)
    arrays = {
        "x": x.reshape(B, S, T, P).transpose(0, 3, 2, 1).reshape(B, P, BW),
        "labels": np.asarray(itok_B_0_2),
        "adapters": np.asarray(itok_B_3_7),
        "thresholds": np.asarray(condB_thresholds),
        "deltas": np.asarray(condB_deltas),
        "zeropoints": np.asarray(condB_zeropoints),
        "w0": tiles_of_weights(L0_cond_W),
        "a0": np.asarray(L0_cond_lora_A).reshape(-1, T, P, R0).transpose(0, 2, 1, 3).reshape(-1, P, T * R0),
        "b0": np.asarray(L0_cond_lora_B_w).T,
        "w2": tiles_of_weights(L2_cond_weight).reshape(-1, 4, 2, P, T * P).transpose(0, 1, 3, 2, 4),
        "b3": np.asarray(L3_cond_B).reshape(-1, R3, T, P).transpose(0, 3, 2, 1).reshape(-1, P, T * R3),
        "a3": np.asarray(L3_cond_A).transpose(0, 2, 1),
    }
    arrays = {name: np.ascontiguousarray(a) for name, a in arrays.items()}
    nc = bacc.Bacc("TRN2", target_bir_lowering=False, num_devices=1, dynamic_dma_scratch_size=1024)
    args = [nc.dram_tensor(name, a.shape, mybir.dt.from_np(a.dtype), kind="ExternalInput").ap()
            for name, a in arrays.items()]
    out = nc.dram_tensor("out", (B, 4, P, CW), F32, kind="ExternalOutput").ap()
    build(nc, *args, out)
    got = run_bass_kernel_spmd(nc, [arrays], core_ids=[0]).results[0]["out"]
    return np.ascontiguousarray(got.reshape(B, 4, P, 2, S).transpose(0, 4, 1, 3, 2)).reshape(B, S, D)
```

```python
from contextlib import ExitStack

import concourse.bass as bass
import numpy as np
from concourse import mybir

ALU = mybir.AluOpType
ACT = mybir.ActivationFunctionType
F32 = mybir.dt.float32
F32R = mybir.dt.float32r
BF16 = mybir.dt.bfloat16
I16 = mybir.dt.int16
I32 = mybir.dt.int32

P = 128
B, S, D = 8, 256, 1024
T = D // P
BW = T * S
UW = BW // 2
CW = BW // 4
QUAD = 32
R0 = 32
R3 = 16
G = 8
TOP_LEVEL = 63.0
ROUND = 12582912.0
CANDS = 3
MASKS = 3
K_SPLIT = 2
K_WHOLE = T - K_SPLIT
STEEP = 2.0 ** 40
BELOW_ONE = 1.0 - 2.0 ** -24
POOL_GROUPS = (1, 2, 3, 4, 5, 6, 7)


def build(nc, x, labels, adapters, thresholds, deltas, zeropoints, w0, a0, b0, w2, b3, a3, out):
    with ExitStack() as ctx:
        def sb(name, shape, dt):
            return ctx.enter_context(nc.sbuf_tensor(name, shape, dt))

        def ps(name, shape):
            return ctx.enter_context(nc.psum_tensor(name, shape, F32))

        def sem(name):
            return ctx.enter_context(nc.semaphore(name))

        w0_hi = sb("w0_hi", [P, T, T * P], F32R)
        w0_lo = sb("w0_lo", [P, T, T * P], F32R)
        w2_sb = sb("w2_sb", [P, T, T * P], F32)
        w2_hi = sb("w2_hi", [P, 2, 2, K_SPLIT * P], F32R)
        w2_lo = sb("w2_lo", [P, 2, 2, K_SPLIT * P], F32R)
        x2_hi = sb("x2_hi", [P, K_SPLIT * S], F32R)
        x2_lo = sb("x2_lo", [P, K_SPLIT * S], F32R)
        x_raw = sb("x_raw", [P, BW], F32)
        x_hi = sb("x_hi", [P, 2, BW], F32R)
        x_lo = sb("x_lo", [P, 2, BW], F32R)
        a0_raw = sb("a0_raw", [P, T, R0], F32)
        a0_split = sb("a0_split", [P, T, 4, R0], F32R)
        b0_split = sb("b0_split", [P, D], F32R)
        low_split = sb("low_split", [P, S], F32R)
        magnitude = sb("magnitude", [P, UW], F32)
        cand = sb("cand", [P, CANDS, UW], F32)
        mask = sb("mask", [P, MASKS, UW], BF16)
        x2 = sb("x2", [P, 2, BW], F32)
        x3 = sb("x3", [P, BW], F32)
        result = sb("result", [P, 2, CW], F32)
        b3_raw = sb("b3_raw", [P, T, R3], F32)
        b3_wide = sb("b3_wide", [P, T, 4, QUAD], F32)
        a3_raw = sb("a3_raw", [P, D], F32)
        a3_split = sb("a3_split", [P, D], F32R)
        bx_split = sb("bx_split", [P, S], F32R)
        ident = sb("ident", [P, P], F32)
        zero = sb("zero", [P, 1], F32)
        table_warmup = sb("table_warmup", [P, 1], F32)
        thr = sb("thr", [P, G], F32)
        delta = sb("delta", [P, G], F32)
        zp = sb("zp", [P, G], F32)
        sorted_thr = sb("sorted_thr", [P, G], F32)
        thr_bias = sb("thr_bias", [P, G], F32)
        inv_delta = sb("inv_delta", [P, G], F32)
        top = sb("top", [P, G], F32)
        lower = sb("lower", [P, G], F32)
        upper = sb("upper", [P, G], F32)
        label_ids = sb("label_ids", [1, B], I32)
        adapter_ids = sb("adapter_ids", [1, B], I32)

        l0_ps = ps("l0_ps", [P, 2, UW])
        l2_ps = ps("l2_ps", [P, 2, CW])
        l3_ps = ps("l3_ps", [P, CW])
        bx_ps = ps("bx_ps", [P, CW])

        ids_loaded = sem("ids_loaded")
        params_loaded = sem("params_loaded")
        b0_loaded = sem("b0_loaded")
        w0_loaded = [sem(f"w0_loaded{o}") for o in range(T)]
        x_loaded = sem("x_loaded")
        a0_loaded = sem("a0_loaded")
        w2_loaded = [sem(f"w2_loaded{q}") for q in range(4)]
        b3_loaded = sem("b3_loaded")
        a3_loaded = sem("a3_loaded")
        out_stored = [sem(f"out_stored{q}") for q in range(4)]
        ident_zeroed = sem("ident_zeroed")
        ident_ready = sem("ident_ready")
        gaps_zeroed = sem("gaps_zeroed")
        param_step = sem("param_step")
        sp_waited = sem("sp_waited")
        dve_waited = sem("dve_waited")
        pool_waited = sem("pool_waited")
        diag_added = sem("diag_added")
        w0_hi_done = sem("w0_hi_done")
        w0_split_done = sem("w0_split_done")
        b0_hi_done = sem("b0_hi_done")
        b0_split_done = sem("b0_split_done")
        x_hi_done = sem("x_hi_done")
        x_split_done = sem("x_split_done")
        a0_hi_done = sem("a0_hi_done")
        a0_split_done = sem("a0_split_done")
        low_done = sem("low_done")
        low_hi_done = sem("low_hi_done")
        low_split_done = sem("low_split_done")
        l0_done = sem("l0_done")
        mag_done = sem("mag_done")
        rounded = sem("rounded")
        masked = sem("masked")
        scaled_dve = sem("scaled_dve")
        scaled_pool = sem("scaled_pool")
        clipped = sem("clipped")
        merged = sem("merged")
        zeroed = sem("zeroed")
        x2_done = sem("x2_done")
        l2_done = sem("l2_done")
        x3_done = sem("x3_done")
        x2_hi_done = sem("x2_hi_done")
        x2_split_done = sem("x2_split_done")
        w2_hi_done = sem("w2_hi_done")
        w2_split_done = sem("w2_split_done")
        last_x2_hi_done = sem("last_x2_hi_done")
        last_x2_split_done = sem("last_x2_split_done")
        last_w2_hi_done = sem("last_w2_hi_done")
        last_w2_split_pool = sem("last_w2_split_pool")
        last_w2_split_done = sem("last_w2_split_done")
        b3_done = sem("b3_done")
        a3_hi_done = sem("a3_hi_done")
        a3_split_done = sem("a3_split_done")
        bx_done = sem("bx_done")
        bx_hi_done = sem("bx_hi_done")
        bx_split_done = sem("bx_split_done")
        l3_done = sem("l3_done")
        out_done = sem("out_done")

        pool_share = len(POOL_GROUPS)
        dve_share = G - pool_share

        def all_steps(engine, step):
            step(0, 0, True, False, False)
            step(1, 1, True, True, False)
            with engine.Fori(1, B // 2 - 1) as pair:
                s = pair * 2
                step(s, 0, True, True, True)
                step(s + 1, 1, True, True, True)
            step(B - 2, 0, True, True, True)
            step(B - 1, 1, True, True, True)
            step(B, 0, False, True, True)
            step(B + 1, 1, False, False, True)

        def first(s):
            return isinstance(s, int) and s == 0

        def has_next(s):
            return not (isinstance(s, int) and s >= B - 1)

        def w2_split_at(s):
            return ((0, 6), (1, 0)) if isinstance(s, int) and s == 1 else ((1, 2), (1, 4))

        def low_rank_at(s):
            if first(s):
                return 0, 6
            return (1, 4) if isinstance(s, int) and s == 1 else (1, 6)

        def l0_unit(s, half):
            if isinstance(s, int) and s == 1 and half == 1:
                return l2_ps[:, :, :].rearrange("p n w -> p (n w)")
            return l0_ps[:, half, :]

        def l2_bank(s, q):
            if isinstance(s, int) and s == 1:
                return l0_ps[:, 1, (q % 2) * CW:(q % 2 + 1) * CW]
            return l2_ps[:, q % 2, :]

        def l3_bank(s, q):
            if isinstance(s, int) and s >= B:
                return l0_ps[:, q // 2, (q % 2) * CW:(q % 2 + 1) * CW]
            return l3_ps[:, :]

        def result_chunk(s, parity, q):
            if isinstance(s, int) and s >= B:
                return x2[:, parity, q * CW:(q + 1) * CW]
            return result[:, q % 2, :]

        block = ctx.enter_context(nc.Block())

        @block.sync
        def _(sp):
            def load_x(n):
                sp.dma_start(x_raw[:, :], x[bass.ds(n, 1)].rearrange("b p w -> p (b w)")).then_inc(x_loaded, 16)

            def load_a0(n):
                label = sp.value_load(label_ids[0:1, bass.ds(n, 1)], min_val=0, max_val=a0.shape[0] - 1)
                sp.dma_start(a0_raw[:, :, :].rearrange("p k r -> p (k r)"),
                             a0[bass.ds(label, 1)].rearrange("l p w -> p (l w)")).then_inc(a0_loaded, 16)

            for q in range(4):
                sp.sem_inc(out_stored[q], 1)
            load_x(0)
            sp.dma_start(w2_sb[:, 0, :], w0[0]).then_inc(w0_loaded[0], 16)
            sp.dma_start(label_ids[:, :], labels.rearrange("(a n) -> a n", a=1)).then_inc(ids_loaded, 16)
            sp.dma_start(adapter_ids[:, :], adapters.rearrange("(a n) -> a n", a=1)).then_inc(ids_loaded, 16)
            sp.dma_start(w2_sb[:, 1, :], w0[1]).then_inc(w0_loaded[1], 16)
            sp.wait_ge(ids_loaded, 2 * 16)
            load_a0(0)
            for q in range(4):
                sp.dma_start(a3_raw[q * QUAD:(q + 1) * QUAD, :], b0).then_inc(b0_loaded, 16)
            sp.dma_start(w2_sb[:, 2, :], w0[2]).then_inc(w0_loaded[2], 16)
            for dst, src in ((thr, thresholds), (delta, deltas), (zp, zeropoints)):
                sp.dma_start(dst[:, :], src.rearrange("(a n) -> a n", a=1).to_broadcast([P, G]))\
                  .then_inc(params_loaded, 16)
            for o in range(3, T):
                sp.dma_start(w2_sb[:, o, :], w0[o]).then_inc(w0_loaded[o], 16)
            sp.wait_ge(x_split_done, 1)
            load_x(1)
            sp.wait_ge(a0_split_done, 1)
            load_a0(1)

            def step(s, parity, stage_a, stage_b, stage_c):
                if stage_a and not first(s) and has_next(s):
                    sp.wait_ge(x_split_done, s + 1)
                    sp.sem_inc(sp_waited, 1)
                    load_x(s + 1)
                    sp.wait_ge(a0_split_done, s + 1)
                    sp.sem_inc(sp_waited, 1)
                    load_a0(s + 1)
                if stage_b:
                    adapter = sp.value_load(adapter_ids[0:1, bass.ds(s - 1, 1)], min_val=0, max_val=b3.shape[0] - 1)
                    if stage_c:
                        sp.wait_ge(b3_done, s - 1)
                        sp.sem_inc(sp_waited, 1)
                        sp.wait_ge(a3_split_done, (s - 1) * 2)
                        sp.sem_inc(sp_waited, 1)
                    else:
                        sp.wait_ge(gaps_zeroed, 2)
                    sp.dma_start(b3_raw[:, :, :].rearrange("p k r -> p (k r)"),
                                 b3[bass.ds(adapter, 1)].rearrange("l p w -> p (l w)")).then_inc(b3_loaded, 16)
                    for q in range(4):
                        sp.dma_start(a3_raw[q * QUAD:q * QUAD + R3, :],
                                     a3[bass.ds(adapter, 1)].rearrange("l r w -> r (l w)")).then_inc(a3_loaded, 16)
                if stage_a:
                    adapter = sp.value_load(adapter_ids[0:1, bass.ds(s, 1)], min_val=0, max_val=b3.shape[0] - 1)
                for q in range(4):
                    if stage_a:
                        if first(s):
                            sp.wait_ge(w0_split_done, 2 * q + 2)
                        else:
                            sp.wait_ge(l2_done, (s - 1) * 4 + (q + 1))
                            sp.sem_inc(sp_waited, 1)
                        sp.dma_start(w2_sb[:, 2 * q:2 * q + 2, :],
                                     w2[bass.ds(adapter, 1), q].rearrange("l p o w -> p (l o) w"))\
                          .then_inc(w2_loaded[q], 16)
                    if stage_c:
                        sp.wait_ge(out_done, (s - 2) * 4 + (q + 1))
                        sp.sem_inc(sp_waited, 1)
                        sp.dma_start(out[bass.ds(s - 2, 1), q].rearrange("b p w -> p (b w)"),
                                     result_chunk(s, parity, q)).then_inc(out_stored[q], 16)

            all_steps(sp, step)
            for q in range(4):
                sp.wait_ge(out_stored[q], 16 * B + 1)

        @block.gpsimd
        def _(pool):
            pool.memset(ident[:, :], 0.0).then_inc(ident_zeroed, 1)
            pool.wait_ge(ident_zeroed, 1)
            pool.affine_select(out=ident[:, :], in_=ident[:, :], compare_op=ALU.not_equal, fill=1.0,
                               base=0, pattern=[[-1, P]], channel_multiplier=1).then_inc(ident_ready, 1)
            pool.memset(zero[:, :], 0.0).then_inc(ident_ready, 1)
            pool.memset(b3_wide[:, :, :, :], 0.0).then_inc(gaps_zeroed, 1)
            pool.wait_ge(b0_split_done, 1)
            pool.memset(a3_raw[:, :], 0.0).then_inc(gaps_zeroed, 1)

            def rescale(s, half, stage_b):
                if stage_b and (half, 0) in w2_split_at(s):
                    split_w2(s, 3)
                for k in POOL_GROUPS:
                    c = cand[:, k % CANDS, :]
                    pool.wait_ge(rounded, (s * 2 + half) * G + (k + 1))
                    pool.sem_inc(pool_waited, 1)
                    pool.tensor_scalar(c, c, -ROUND, delta[:, k:k + 1], ALU.add, ALU.mult)\
                        .then_inc(scaled_pool, 1)
                    if stage_b and (half, k) in w2_split_at(s):
                        split_w2(s, 2 + w2_split_at(s).index((half, k)))

            def split_w2(s, q):
                pool.wait_ge(w2_hi_done, (s - 1) * 4 + (q + 1))
                pool.sem_inc(pool_waited, 1)
                pool.tensor_tensor(w2_lo[:, q % 2, :, :], w2_sb[:, 2 * q:2 * q + 2, K_WHOLE * P:],
                                   w2_hi[:, q % 2, :, :].bitcast(F32), ALU.subtract).then_inc(w2_split_done, 1)

            def step(s, parity, stage_a, stage_b, stage_c):
                if stage_a and stage_b:
                    split_w2(s, 0)
                    split_w2(s, 1)
                if stage_c:
                    pool.wait_ge(b3_loaded, (s - 1) * 16)
                    if not stage_b:
                        pool.wait_ge(bx_done, s - 2)
                    pool.sem_inc(pool_waited, 1)
                    pool.tensor_copy(b3_wide[:, :, :, 0:R3],
                                     b3_raw[:, :, :].unsqueeze(2).to_broadcast([P, T, 4, R3])).then_inc(b3_done, 1)
                    if not stage_a and stage_b:
                        for o in range(2):
                            pool.wait_ge(last_w2_hi_done, o + 1)
                            pool.tensor_tensor(w0_lo[:, o, :], w2_sb[:, o, :], w0_hi[:, o, :].bitcast(F32),
                                               ALU.subtract).then_inc(last_w2_split_pool, 1)
                    pool.wait_ge(a3_hi_done, s - 1)
                    pool.wait_ge(b3_done, s - 1)
                    if not stage_a:
                        pool.wait_ge(last_w2_split_pool, 2)
                    for n, q in enumerate((1, 3)):
                        rows = slice(q * QUAD, q * QUAD + R3)
                        pool.tensor_tensor(a3_split[rows, :], a3_raw[rows, :],
                                           a3_split[rows, :].bitcast(F32), ALU.subtract)\
                            .then_inc(a3_split_done, 1)
                        pool.wait_ge(a3_split_done, (s - 2) * 2 + (n + 1))
                if stage_a:
                    rescale(s, 0, stage_b)
                    rescale(s, 1, stage_b)

            pool.wait_ge(params_loaded, 3 * 16)
            all_steps(pool, step)

        @block.scalar
        def _(act):
            def split_w0(o):
                act.wait_ge(diag_added, o + 1)
                act.activation(w0_hi[:, o, :], w2_sb[:, o, :], ACT.Copy).then_inc(w0_hi_done, 1)

            def split_batch(s, parity):
                act.wait_ge(x_loaded, (s + 1) * 16)
                act.activation(x_hi[:, parity, :], x_raw[:, :], ACT.Copy).then_inc(x_hi_done, 1)
                if first(s):
                    split_w0(0)
                act.wait_ge(a0_loaded, (s + 1) * 16)
                act.activation(a0_split[:, :, :, :], a0_raw[:, :, :].unsqueeze(2).to_broadcast([P, T, 4, R0]),
                               ACT.Copy).then_inc(a0_hi_done, 1)

            def low_rank_hi(s):
                act.wait_ge(low_done, s + 1)
                if not first(s):
                    act.wait_ge(l0_done, s * 2)
                act.activation(low_split[:, :], bx_ps[:, 0:S], ACT.Copy).then_inc(low_hi_done, 1)

            act.wait_ge(ident_ready, 2)
            act.activation(table_warmup[:, :], zero[:, :], ACT.Abs)
            split_batch(0, 0)
            for o in range(T):
                if o > 0:
                    split_w0(o)
                else:
                    act.wait_ge(b0_loaded, 4 * 16)
                    act.activation(b0_split[:, :], a3_raw[:, :], ACT.Copy, scale=0.5).then_inc(b0_hi_done, 1)
                if o == 1:
                    low_rank_hi(0)

            def split_bx(s):
                act.wait_ge(bx_done, s - 1)
                act.activation(bx_split[:, :], bx_ps[:, 0:S], ACT.Copy).then_inc(bx_hi_done, 1)

            def split_x2(s, parity):
                if not (isinstance(s, int) and s == 1):
                    act.wait_ge(l2_done, (s - 1) * 4)
                act.wait_ge(x2_done, s * 2)
                act.activation(x2_hi[:, :], x2[:, 1 - parity, K_WHOLE * S:], ACT.Copy).then_inc(x2_hi_done, 1)

            def split_w2(s, q):
                if not (isinstance(s, int) and s == 1 and q < 2):
                    act.wait_ge(l2_done, (s - 1) * 4 + (q - 1))
                act.wait_ge(w2_loaded[q], s * 16)
                act.activation(w2_hi[:, q % 2, :, :], w2_sb[:, 2 * q:2 * q + 2, K_WHOLE * P:], ACT.Copy)\
                   .then_inc(w2_hi_done, 1)

            def last_split_w2(o):
                act.wait_ge(w2_loaded[o // 2], 16 * B)
                act.activation(w0_hi[:, o, :], w2_sb[:, o, :], ACT.Copy).then_inc(last_w2_hi_done, 1)

            def quantise(s, half, parity, stage_b, stage_c):
                unit = s * 2 + half
                src = l0_unit(s, half)
                act.wait_ge(l0_done, 4 if isinstance(s, int) and s == 1 else unit + 1)
                if not (first(s) and half == 0):
                    act.wait_ge(masked, unit * G)
                act.activation(magnitude[:, :], src, ACT.Abs).then_inc(mag_done, 1)

                def candidate(k):
                    if k >= CANDS:
                        act.wait_ge(merged, unit * G + (k - CANDS + 1))
                    elif not (first(s) and half == 0):
                        act.wait_ge(merged, unit * G - (G - 1 - k) % CANDS)
                    act.activation(cand[:, k % CANDS, :], src, ACT.Identity, bias=ROUND,
                                   scale=inv_delta[:, k:k + 1]).then_inc(rounded, 1)

                def test(j):
                    if j >= MASKS:
                        act.wait_ge(merged, unit * G + (j - MASKS + 2))
                    elif not (first(s) and half == 0):
                        if j == 0:
                            act.wait_ge(merged, unit * G)
                        elif j == 1:
                            act.wait_ge(zeroed, unit)
                    act.activation(mask[:, j % MASKS, :], magnitude[:, :], ACT.Relu, bias=thr_bias[:, j:j + 1],
                                   scale=-STEEP * BELOW_ONE).then_inc(masked, 1)

                if stage_b and (half, 0) in w2_split_at(s):
                    split_w2(s, 3)
                candidate(0)
                candidate(1)
                if half == 0 and stage_b:
                    split_x2(s, parity)
                act.wait_ge(mag_done, unit + 1)
                for k in range(2, G):
                    test(k - 2)
                    candidate(k)
                    if k == 2 and half == 0 and stage_c:
                        split_bx(s)
                    if stage_b and (half, k) in w2_split_at(s):
                        split_w2(s, 2 + w2_split_at(s).index((half, k)))
                    if first(s) and half == 0 and k == 3:
                        split_batch(1, 1)
                    if (half, k) == low_rank_at(s) and has_next(s):
                        low_rank_hi(s + 1)
                test(G - 2)
                test(G - 1)

            def step(s, parity, stage_a, stage_b, stage_c):
                if stage_c:
                    act.wait_ge(a3_loaded, (s - 1) * 64)
                    if not stage_b:
                        act.wait_ge(l3_done, (s - 2) * 4)
                    else:
                        act.wait_ge(l2_done, (s - 1) * 4)
                    act.activation(a3_split[:, :], a3_raw[:, :], ACT.Copy).then_inc(a3_hi_done, 1)
                    if not stage_b:
                        split_bx(s)
                if stage_b and not stage_a:
                    act.wait_ge(l0_done, 2 * B)
                    for half in range(2):
                        cols = slice(half * UW, (half + 1) * UW)
                        last_split_w2(half)
                        act.wait_ge(x2_done, 2 * B - 1 + half)
                        act.activation(x_hi[:, 1 - parity, cols], x2[:, 1 - parity, cols], ACT.Copy)\
                           .then_inc(last_x2_hi_done, 1)
                    split_bx(s)
                    for o in range(2, T):
                        last_split_w2(o)
                if stage_a:
                    if stage_b:
                        split_w2(s, 0)
                        split_w2(s, 1)
                    quantise(s, 0, parity, stage_b, stage_c)
                    if not first(s) and has_next(s):
                        act.wait_ge(l0_done, s * 2)
                        split_batch(s + 1, 1 - parity)
                    quantise(s, 1, parity, stage_b, stage_c)

            act.wait_ge(param_step, 6)
            all_steps(act, step)

        @block.vector
        def _(dve):
            def split_batch(s, parity):
                dve.wait_ge(x_hi_done, s + 1)
                dve.tensor_tensor(x_lo[:, parity, :], x_raw[:, :], x_hi[:, parity, :].bitcast(F32),
                                  ALU.subtract).then_inc(x_split_done, 1)
                if first(s):
                    split_w0(0)
                dve.wait_ge(a0_hi_done, s + 1)
                dve.tensor_tensor(a0_split[:, :, 2, :], a0_raw[:, :, :], a0_split[:, :, 2, :].bitcast(F32),
                                  ALU.subtract).then_inc(a0_split_done, 1)

            def low_rank_lo(s):
                rows = slice(3 * QUAD, 4 * QUAD)
                dve.wait_ge(low_hi_done, s + 1)
                dve.tensor_tensor(low_split[rows, :], bx_ps[rows, 0:S], low_split[rows, :].bitcast(F32),
                                  ALU.subtract).then_inc(low_split_done, 1)

            dve.wait_ge(ident_ready, 2)

            def add_diag(o):
                dve.wait_ge(w0_loaded[o], 16)
                d = w2_sb[:, o, o * P:(o + 1) * P]
                dve.tensor_tensor(d, d, ident[:, :], ALU.add).then_inc(diag_added, 1)

            def split_w0(o):
                if o + 1 < T:
                    add_diag(o + 1)
                dve.wait_ge(w0_hi_done, o + 1)
                dve.tensor_tensor(w0_lo[:, o, :], w2_sb[:, o, :], w0_hi[:, o, :].bitcast(F32),
                                  ALU.subtract).then_inc(w0_split_done, 1)

            add_diag(0)
            split_batch(0, 0)
            for o in range(T):
                if o > 0:
                    split_w0(o)
                else:
                    rows = slice(QUAD, 2 * QUAD)
                    dve.wait_ge(b0_hi_done, 1)
                    dve.scalar_tensor_tensor(b0_split[rows, :], a3_raw[rows, :], 0.5,
                                             b0_split[rows, :].bitcast(F32), ALU.mult, ALU.subtract)\
                        .then_inc(b0_split_done, 1)
                if o == 1:
                    low_rank_lo(0)

            def split_w2(o):
                dve.wait_ge(last_w2_hi_done, o + 1)
                dve.tensor_tensor(w0_lo[:, o, :], w2_sb[:, o, :], w0_hi[:, o, :].bitcast(F32), ALU.subtract)\
                   .then_inc(last_w2_split_done, 1)

            def split_bx(s):
                rows = slice(2 * QUAD, 4 * QUAD)
                dve.wait_ge(bx_hi_done, s - 1)
                dve.tensor_tensor(bx_split[rows, :], bx_ps[rows, 0:S], bx_split[rows, :].bitcast(F32),
                                  ALU.subtract).then_inc(bx_split_done, 1)

            dve.wait_ge(params_loaded, 3 * 16)
            dve.max(sorted_thr[:, :], thr[:, :]).then_inc(param_step, 1)
            dve.reciprocal(inv_delta[:, :], delta[:, :]).then_inc(param_step, 1)
            dve.tensor_scalar(top[:, :], zp[:, :], -1.0, TOP_LEVEL, ALU.mult, ALU.add).then_inc(param_step, 1)
            dve.scalar_tensor_tensor(lower[:, :], zp[:, :], -1.0, delta[:, :], ALU.mult, ALU.mult)\
                .then_inc(param_step, 1)
            dve.wait_ge(param_step, 3)
            dve.tensor_tensor(upper[:, :], top[:, :], delta[:, :], ALU.mult).then_inc(param_step, 1)
            dve.tensor_scalar(thr_bias[:, :], sorted_thr[:, :], STEEP, 1e-30, ALU.mult, ALU.add)\
                .then_inc(param_step, 1)
            dve.wait_ge(param_step, 6)

            def finish_chunk(s, parity, q, stage_c):
                cols = slice(q * CW, (q + 1) * CW)
                if stage_c:
                    if not (isinstance(s, int) and s >= B):
                        if q < 2:
                            dve.wait_ge(out_stored[q + 2], (s - 2) * 16 + 1)
                        else:
                            dve.wait_ge(out_stored[q - 2], (s - 1) * 16 + 1)
                    dve.wait_ge(l3_done, (s - 2) * 4 + (q + 1))
                    dve.tensor_tensor(result_chunk(s, parity, q), l3_bank(s, q), x3[:, cols], ALU.add)\
                       .then_inc(out_done, 1)

            def drain_chunk(s, parity, q, stage_b, stage_c):
                cols = slice(q * CW, (q + 1) * CW)
                if stage_b:
                    if stage_c:
                        dve.wait_ge(out_done, (s - 2) * 4 + (q + 1))
                    dve.wait_ge(l2_done, (s - 1) * 4 + (q + 1))
                    dve.tensor_tensor(x3[:, cols], l2_bank(s, q), x2[:, 1 - parity, cols],
                                      ALU.add).then_inc(x3_done, 1)

            def split_x2(s, parity):
                dve.wait_ge(x2_hi_done, s)
                dve.tensor_tensor(x2_lo[:, :], x2[:, 1 - parity, K_WHOLE * S:], x2_hi[:, :].bitcast(F32),
                                  ALU.subtract).then_inc(x2_split_done, 1)

            def quantise(s, half, parity, stage_b, stage_c):
                unit = s * 2 + half
                y = x2[:, parity, half * UW:(half + 1) * UW]

                def scale(k):
                    if k not in POOL_GROUPS:
                        c = cand[:, k % CANDS, :]
                        dve.wait_ge(rounded, unit * G + (k + 1))
                        dve.tensor_scalar(c, c, -ROUND, delta[:, k:k + 1], ALU.add, ALU.mult)\
                            .then_inc(scaled_dve, 1)

                def clip(k):
                    c = cand[:, k % CANDS, :]
                    before = sum(1 for n in POOL_GROUPS if n < k)
                    if k in POOL_GROUPS:
                        dve.wait_ge(scaled_pool, unit * pool_share + (before + 1))
                    else:
                        dve.wait_ge(scaled_dve, unit * dve_share + (k - before + 1))
                    if k == 0:
                        dve.tensor_scalar(y, c, lower[:, k:k + 1], upper[:, k:k + 1], ALU.max, ALU.min)\
                            .then_inc(merged, 1)
                    else:
                        dve.tensor_scalar(c, c, lower[:, k:k + 1], upper[:, k:k + 1], ALU.max, ALU.min)\
                            .then_inc(clipped, 1)

                def merge(k):
                    dve.wait_ge(masked, unit * G + k)
                    dve.wait_ge(clipped, unit * (G - 1) + k)
                    dve.sem_inc(dve_waited, 1)
                    dve.copy_predicated(y, mask[:, (k - 1) % MASKS, :].bitcast(I16), cand[:, k % CANDS, :])\
                        .then_inc(merged, 1)

                drain_at = ((0, G), (1, 3), (1, 5), (1, G)) if stage_c else ((0, 6), (0, G), (1, 2), (1, 5))
                finish_at = ((0, 5), (0, G), (1, 3), (1, 5))

                def chunks_after(k):
                    for q in range(4):
                        if drain_at[q] == (half, k):
                            drain_chunk(s, parity, q, stage_b, stage_c)
                        if finish_at[q] == (half, k):
                            finish_chunk(s, parity, q, stage_c)

                if not (isinstance(s, int) and s < 2):
                    dve.wait_ge(x3_done, (s - 1) * 4)
                scale(0)
                scale(1)
                clip(0)
                clip(1)
                if half == 0 and stage_b:
                    split_x2(s, parity)
                for k in range(2, G):
                    scale(k)
                    dve.wait_ge(merged, unit * G + (k - 1))
                    merge(k - 1)
                    clip(k)
                    if k == 3 and half == 0 and stage_c:
                        split_bx(s)
                    chunks_after(k)
                    if first(s) and half == 0 and k == 3:
                        split_batch(1, 1)
                    if (half, k) == low_rank_at(s) and has_next(s):
                        low_rank_lo(s + 1)
                dve.wait_ge(merged, unit * G + (G - 1))
                merge(G - 1)
                chunks_after(G)
                dve.wait_ge(masked, unit * G + G)
                dve.wait_ge(merged, unit * G + G)
                dve.sem_inc(dve_waited, 1)
                dve.copy_predicated(y, mask[:, (G - 1) % MASKS, :].bitcast(I16), zero[:, :].to_broadcast([P, UW]))\
                    .then_inc(zeroed, 1)
                dve.wait_ge(zeroed, unit + 1)
                dve.tensor_tensor(y, l0_unit(s, half), y, ALU.add).then_inc(x2_done, 1)

            def step(s, parity, stage_a, stage_b, stage_c):
                if stage_a:
                    quantise(s, 0, parity, stage_b, stage_c)
                    if not first(s) and has_next(s):
                        split_batch(s + 1, 1 - parity)
                    quantise(s, 1, parity, stage_b, stage_c)
                else:
                    if stage_b:
                        for half in range(2):
                            cols = slice(half * UW, (half + 1) * UW)
                            dve.wait_ge(last_x2_hi_done, half + 1)
                            dve.tensor_tensor(x_lo[:, 1 - parity, cols], x2[:, 1 - parity, cols],
                                              x_hi[:, 1 - parity, cols].bitcast(F32), ALU.subtract)\
                               .then_inc(last_x2_split_done, 1)
                    split_bx(s)
                    if stage_b:
                        split_w2(2)
                        split_w2(3)
                    for q in range(4):
                        finish_chunk(s, parity, q, stage_c)
                    drain_chunk(s, parity, 0, stage_b, stage_c)
                    for q in range(1, 4):
                        if stage_b and q < 3:
                            split_w2(2 * q + 2)
                            split_w2(2 * q + 3)
                        drain_chunk(s, parity, q, stage_b, stage_c)

            all_steps(dve, step)

        @block.tensor
        def _(pe):
            def layer0(s, parity, half, tiles):
                for i in tiles:
                    o = half * (T // 2) + i
                    dst = l0_unit(s, half)[:, i * S:(i + 1) * S]
                    if i == 0 and not first(s) and not (isinstance(s, int) and s == 1 and half == 1):
                        pe.wait_ge(x2_done, s * 2 + (half - 1))
                    if first(s):
                        pe.wait_ge(w0_hi_done, o + 1)
                        if i == 0:
                            pe.wait_ge(x_hi_done, 1)
                    start = True
                    for w, v in ((w0_hi, x_hi), (w0_hi, x_lo), (w0_lo, x_hi)):
                        if first(s) and w is w0_lo:
                            pe.wait_ge(w0_split_done, o + 1)
                        if first(s) and o == 0 and v is x_lo:
                            pe.wait_ge(x_split_done, 1)
                        for k in range(T):
                            nc.tensor.matmul(dst, w[:, o, k * P:(k + 1) * P], v[:, parity, k * S:(k + 1) * S],
                                             start=start, stop=False)
                            start = False
                    if first(s) and o == 0:
                        low_rank0(0, 0)
                    if i == 0:
                        pe.wait_ge(low_split_done, s + 1)
                        if first(s):
                            pe.wait_ge(b0_split_done, 1)
                    last = nc.tensor.matmul(dst, b0_split[:, o * P:(o + 1) * P], low_split[:, :],
                                            start=False, stop=True)
                if i == T // 2 - 1:
                    last.then_inc(l0_done, 1)

            def low_rank0(s, parity):
                pe.wait_ge(x_split_done, s + 1)
                pe.wait_ge(a0_split_done, s + 1)
                for v in (x_hi, x_lo):
                    for k in range(T):
                        last = nc.tensor.matmul(bx_ps[:, 0:S], a0_split[:, k, :, :].rearrange("p q r -> p (q r)"),
                                                v[:, parity, k * S:(k + 1) * S],
                                                start=(v is x_hi and k == 0), stop=(v is x_lo and k == T - 1))
                last.then_inc(low_done, 1)

            def low_rank3(s, parity):
                pe.wait_ge(b3_done, s - 1)
                for k in range(T):
                    if k % 2 == 0:
                        pe.wait_ge(x3_done, (s - 2) * 4 + (k // 2 + 1))
                    last = nc.tensor.matmul(bx_ps[:, 0:S], b3_wide[:, k, :, :].rearrange("p q r -> p (q r)"),
                                            x3[:, k * S:(k + 1) * S], start=(k == 0), stop=(k == T - 1))
                last.then_inc(bx_done, 1)

            def layer3(s, q, shared_bank):
                if q == 0:
                    pe.wait_ge(bx_split_done, s - 1)
                    pe.wait_ge(a3_split_done, (s - 1) * 2)
                if shared_bank:
                    pe.wait_ge(out_done, (s - 2) * 4 + q)
                for i in range(2):
                    o = 2 * q + i
                    last = nc.tensor.matmul(l3_bank(s, q)[:, i * S:(i + 1) * S], a3_split[:, o * P:(o + 1) * P],
                                            bx_split[:, :], start=True, stop=True)
                last.then_inc(l3_done, 1)

            def last_layer2(parity, dst, o):
                for w, v, v_done in ((w0_hi, x_hi, last_x2_hi_done), (w0_lo, x_hi, last_x2_hi_done),
                                     (w0_hi, x_lo, last_x2_split_done)):
                    if w is w0_hi:
                        pe.wait_ge(last_w2_hi_done, o + 1)
                    elif o < 2:
                        pe.wait_ge(last_w2_split_pool, o + 1)
                    else:
                        pe.wait_ge(last_w2_split_done, o - 1)
                    for k in range(T):
                        if o == 0 and k % (T // 2) == 0:
                            pe.wait_ge(v_done, k // (T // 2) + 1)
                        last = nc.tensor.matmul(dst, w[:, o, k * P:(k + 1) * P], v[:, 1 - parity, k * S:(k + 1) * S],
                                                start=(v is x_hi and w is w0_hi and k == 0),
                                                stop=(v is x_lo and k == T - 1))
                return last

            def layer2(s, parity, q):
                pe.wait_ge(w2_loaded[q], s * 16)
                if q == 0:
                    pe.wait_ge(x2_done, s * 2)
                if not (isinstance(s, int) and s == 1 and q < 2):
                    pe.wait_ge(x3_done, (s - 1) * 4 + (q - 1))
                for i in range(2):
                    o = 2 * q + i
                    dst = l2_bank(s, q)[:, i * S:(i + 1) * S]
                    if isinstance(s, int) and s == B:
                        last = last_layer2(parity, dst, o)
                        continue
                    for k in range(K_WHOLE):
                        nc.tensor.matmul(dst, w2_sb[:, o, k * P:(k + 1) * P], x2[:, 1 - parity, k * S:(k + 1) * S],
                                         start=(k == 0), stop=False)
                    if i == 0:
                        pe.wait_ge(w2_split_done, (s - 1) * 4 + (q + 1))
                        if q == 0:
                            pe.wait_ge(x2_split_done, s)
                    for w, v in ((w2_hi, x2_hi), (w2_lo, x2_hi), (w2_hi, x2_lo)):
                        for k in range(K_SPLIT):
                            last = nc.tensor.matmul(dst, w[:, q % 2, i, k * P:(k + 1) * P], v[:, k * S:(k + 1) * S],
                                                    start=False, stop=(v is x2_lo and k == K_SPLIT - 1))
                last.then_inc(l2_done, 1)

            def step(s, parity, stage_a, stage_b, stage_c):
                if isinstance(s, int) and s == 1:
                    layer0(s, parity, 1, range(4))
                if stage_a:
                    layer0(s, parity, 0, range(4))
                if stage_c:
                    low_rank3(s, parity)
                if stage_a and not (isinstance(s, int) and s == 1):
                    layer0(s, parity, 1, range(4))
                if stage_a:
                    for q in range(4):
                        if q == 3 and has_next(s):
                            low_rank0(s + 1, 1 - parity)
                        if stage_c:
                            layer3(s, q, q > 0)
                        if stage_b:
                            layer2(s, parity, q)
                else:
                    if stage_b:
                        layer2(s, parity, 0)
                    for q in range(4):
                        layer3(s, q, False)
                    if stage_b:
                        for q in range(1, 4):
                            layer2(s, parity, q)

            all_steps(pe, step)


def kernel(x, itok_B_0_2, condB_thresholds, condB_deltas, condB_zeropoints, itok_B_3_7, L0_cond_W,
           L0_cond_lora_A, L0_cond_lora_B_w, L2_cond_weight, L3_cond_A, L3_cond_B):
    import concourse.bacc as bacc
    from concourse.bass_utils import run_bass_kernel_spmd

    def tiles_of_weights(w):
        w = np.asarray(w)
        lead = w.shape[:-2]
        n = len(lead)
        w = w.reshape(*lead, T, P, T, P)
        return np.ascontiguousarray(w.transpose(*range(n), n, n + 3, n + 2, n + 1)).reshape(*lead, T, P, T * P)

    x = np.asarray(x)
    arrays = {
        "x": x.reshape(B, S, T, P).transpose(0, 3, 2, 1).reshape(B, P, BW),
        "labels": np.asarray(itok_B_0_2),
        "adapters": np.asarray(itok_B_3_7),
        "thresholds": np.asarray(condB_thresholds),
        "deltas": np.asarray(condB_deltas),
        "zeropoints": np.asarray(condB_zeropoints),
        "w0": tiles_of_weights(L0_cond_W),
        "a0": np.asarray(L0_cond_lora_A).reshape(-1, T, P, R0).transpose(0, 2, 1, 3).reshape(-1, P, T * R0),
        "b0": np.asarray(L0_cond_lora_B_w).T,
        "w2": tiles_of_weights(L2_cond_weight).reshape(-1, 4, 2, P, T * P).transpose(0, 1, 3, 2, 4),
        "b3": np.asarray(L3_cond_B).reshape(-1, R3, T, P).transpose(0, 3, 2, 1).reshape(-1, P, T * R3),
        "a3": np.asarray(L3_cond_A).transpose(0, 2, 1),
    }
    arrays = {name: np.ascontiguousarray(a) for name, a in arrays.items()}
    nc = bacc.Bacc("TRN2", target_bir_lowering=False, num_devices=1, dynamic_dma_scratch_size=1024)
    args = [nc.dram_tensor(name, a.shape, mybir.dt.from_np(a.dtype), kind="ExternalInput").ap()
            for name, a in arrays.items()]
    out = nc.dram_tensor("out", (B, 4, P, CW), F32, kind="ExternalOutput").ap()
    build(nc, *args, out)
    got = run_bass_kernel_spmd(nc, [arrays], core_ids=[0]).results[0]["out"]
    return np.ascontiguousarray(got.reshape(B, 4, P, 2, S).transpose(0, 4, 1, 3, 2)).reshape(B, S, D)
```
